# Optimizing a Trainium2 kernel written in Bass

```python
import numpy as np
import jax
import jax.numpy as jnp

def _softmax(x, axis=-1):
    return jax.nn.softmax(x, axis=axis)

def _gelu(x):
    return jax.nn.gelu(x, approximate=True)

def _silu(x):
    return jax.nn.silu(x)

def _sigmoid(x):
    return jax.nn.sigmoid(x)

def _layernorm(x, axis=-1, eps=1e-05):
    m = jnp.mean(x, axis=axis, keepdims=True)
    v = jnp.var(x, axis=axis, keepdims=True)
    return (x - m) / jnp.sqrt(v + eps)

def _scatter_add(tgt, idx, src, axis=0):
    return tgt.at[idx].add(src)

def _segment_sum(src, seg, n):
    return jax.ops.segment_sum(src, seg, n)
kernel_name = 'mk_cond_resid_d2_seqx_r8_a53334'

def setup_inputs(seed: int=0):
    np.random.seed(seed)
    _w = jnp.asarray

    def _rec_inputs():
        import jax
        import jax.numpy as jnp
        _rk = jax.random.key(seed)
        x = 7.22e-05 + 1 * jax.random.normal(jax.random.fold_in(_rk, 1), (32, 32, 512), jnp.float32)
        _lenS = 32 - jax.random.randint(jax.random.fold_in(_rk, 7), (32,), 0, max(1, 32 // 4) + 1, jnp.int32)
        _lenS2 = 32 - jax.random.randint(jax.random.fold_in(_rk, 8), (32,), 0, max(1, 32 // 4) + 1, jnp.int32)
        condB_coeff = 0.00219231 + 0.0100837 * jax.random.normal(jax.random.fold_in(_rk, 11), (32,), jnp.float32)
        itok_B_0_15 = jax.random.randint(jax.random.fold_in(_rk, 13), (32,), 0, 16, jnp.int32)
        _validS = jnp.arange(32)[None, :] < _lenS[:, None]
        _validS2 = jnp.arange(32)[None, :] < _lenS2[:, None]
        _causal = jnp.tril(jnp.ones((32, 32), dtype=bool))
        mask_Bx4096x4096_ik1 = jnp.where(jnp.ones((32, 512, 512), dtype=bool), 1, 0).astype(jnp.int32)
        return (x, condB_coeff, itok_B_0_15, mask_Bx4096x4096_ik1)
    x, condB_coeff, itok_B_0_15, mask_Bx4096x4096_ik1 = _rec_inputs()

    def _L0_cond_setup():
        import jax, jax.numpy as jnp
        import numpy as np
        B, S, D_IN, D_OUT = (4, 64, 512, 512)
        key = jax.random.key(seed)
        k1, k2, k3, k4, k5 = jax.random.split(key, 5)
        hidden_states = jax.random.normal(k1, (B, S, D_IN), dtype=jnp.float32)
        W = jax.random.normal(k2, (D_OUT, D_IN), dtype=jnp.float32) * 0.02
        b = jax.random.normal(k3, (D_OUT,), dtype=jnp.float32) * 0.02
        coeff = jax.random.normal(k4, (B,), dtype=jnp.float32) * 0.01
        mask = jax.random.randint(k5, (B, D_IN, D_OUT), 0, 2, dtype=jnp.int32)
        return {'hidden_states': hidden_states, 'W': W, 'b': b, 'coeff': coeff, 'mask': mask}
    _L0_cond_all = _L0_cond_setup()
    _L0_cond_in = {k: v for k, v in _L0_cond_all.items() if k in ('W', 'b')}
    del _L0_cond_all

    def _L1_cond_setup():
        import jax, jax.numpy as jnp
        import numpy as np
        NUM_CONDITIONS = 16
        IN_CH = 32
        OUT_CH = 32
        B = 64
        T = 512
        key = jax.random.key(seed)
        k_x, k_w, k_c = jax.random.split(key, 3)
        x = jax.random.normal(k_x, (B, IN_CH, T), dtype=jnp.float32)
        bound = float(np.sqrt(6.0 / IN_CH))
        weights = jax.random.uniform(k_w, (NUM_CONDITIONS, IN_CH, OUT_CH), dtype=jnp.float32, minval=-bound, maxval=bound)
        condition = jax.random.randint(k_c, (B,), 0, NUM_CONDITIONS, dtype=jnp.int64)
        return {'x': x, 'weights': weights, 'condition': condition}
    _L1_cond_all = _L1_cond_setup()
    _L1_cond_in = {k: v for k, v in _L1_cond_all.items() if k in ('weights',)}
    del _L1_cond_all
    return {'x': x, 'condB_coeff': condB_coeff, 'itok_B_0_15': itok_B_0_15, 'mask_Bx4096x4096_ik1': mask_Bx4096x4096_ik1, 'L0_cond_W': _L0_cond_in['W'], 'L0_cond_b': _L0_cond_in['b'], 'L1_cond_weights': _L1_cond_in['weights']}

def reference(x, condB_coeff, itok_B_0_15, mask_Bx4096x4096_ik1, L0_cond_W, L0_cond_b, L1_cond_weights):
    import jax
    import jax.numpy as jnp

    def _L0_cond_ref(hidden_states, W, b, coeff, mask):
        import jax, jax.numpy as jnp
        import numpy as np
        B, S, D_IN, D_OUT = (4, 64, 512, 512)
        output = jnp.einsum('bsi,oi->bso', hidden_states, W) + b
        sign = (2 * mask - 1).astype(hidden_states.dtype)
        diff = jnp.einsum('bsi,bio->bso', hidden_states, sign)
        return output + diff * coeff[:, None, None]

    def _L1_cond_ref(x, weights, condition):
        import jax, jax.numpy as jnp
        import numpy as np
        NUM_CONDITIONS = 16
        IN_CH = 32
        OUT_CH = 32
        B = 64
        T = 512
        W = weights[condition]
        return jnp.einsum('bct,bcd->bdt', x, W)
    x = x + _L0_cond_ref(x, L0_cond_W, L0_cond_b, condB_coeff, mask_Bx4096x4096_ik1)
    x = x + _L1_cond_ref(x, L1_cond_weights, itok_B_0_15)
    return x

_drawn_inputs = setup_inputs


def setup_inputs(seed=0):
    import zlib

    import numpy as np

    out = dict(_drawn_inputs(seed))
    spreads = {}
    factors = {'L0_cond_b': 3.126}
    for name, (base, spread) in spreads.items():
        noise = np.random.default_rng([zlib.crc32(name.encode()), seed]).standard_normal(out[name].shape)
        drawn = base * np.exp(spread * noise) if base else spread * noise
        out[name] = jnp.asarray(drawn.astype(out[name].dtype))
    for name, factor in factors.items():
        out[name] = (out[name] * factor).astype(out[name].dtype)
    return out
```

```python
from contextlib import ExitStack

import concourse.bass as bass
from concourse import mybir

F32 = mybir.dt.float32
I32 = mybir.dt.int32
ALU = mybir.AluOpType
ACT = mybir.ActivationFunctionType
AX_X = mybir.AxisListType.X

P = 128


def cond_resid_kernel(
    nc: bass.Bass,
    x: bass.AP,
    coeff: bass.AP,
    cond: bass.AP,
    mask: bass.AP,
    W: bass.AP,
    bias: bass.AP,
    weights: bass.AP,
    out: bass.AP,
):
    B, S, D = x.shape
    NCOND, C, _ = weights.shape
    T = D // P
    BG = P // S
    G = B // BG
    CJ = P // C
    J = NCOND // CJ
    LAST = G - 1
    PIECES = [(0, D // 2), (D // 2, D // 4), (3 * D // 4, D // 4)]
    ACT_B = (0, 2)
    DVE_B = (1, 3)
    assert S == C and BG * S == P and T * P == D and G % 2 == 0 and J * CJ == NCOND

    x_v = x.rearrange("(g b) s d -> g (b s) d", b=BG)
    out_v = out.rearrange("(g b) s d -> g (b s) d", b=BG)
    mask_v = mask.rearrange("b (p t) o -> b p t o", t=T)
    w_v = W.rearrange("(q o) i -> o q i", o=P)
    cw_v = weights.rearrange("(j k) c d -> (k c) j d", j=J)

    with ExitStack() as ctx:
        def sb(name, shape, dt=F32):
            return ctx.enter_context(nc.sbuf_tensor(name, shape, dt))

        def pb(name, shape):
            return ctx.enter_context(nc.psum_tensor(name, shape, F32))

        def sem(name):
            return ctx.enter_context(nc.semaphore(name))

        raw = sb("raw", [P, 2 * BG, T, D], I32)
        sgn = sb("sgn", [P, 2 * BG, T, D])
        x_in = sb("x_in", [P, 2, D])
        xT = sb("xT", [P, 2, T, P])
        xsT = sb("xsT", [P, 2, T, P])
        xb = sb("xb", [P, D])
        x1 = sb("x1", [P, D])
        y = sb("y", [P, D])
        w_in = sb("w_in", [P, T, D])
        wT = sb("wT", [P, T, D])
        cw = sb("cw", [P, J, C])
        sel = sb("sel", [P, J, P])
        bd = sb("bd", [P, P])
        ident = sb("ident", [P, P])
        ident_c = sb("ident_c", [P, C])
        blocks = sb("blocks", [P, BG])
        ones = sb("ones", [1, P])
        bias_row = sb("bias_row", [1, D])
        bias_all = sb("bias_all", [P, D])
        coeff_all = sb("coeff_all", [P, B])
        cond_all = sb("cond_all", [P, B], I32)
        wrap = sb("wrap", [P, B])
        cond_f = sb("cond_f", [P, B])
        kq = sb("kq", [P, 1])
        hit = sb("hit", [P, J, B])

        acc = pb("acc", [P, D])
        trp = pb("trp", [P, T, P])
        pick = pb("pick", [P, D])
        mix = pb("mix", [P, D])
        side = [pb(f"side{n}", [P, D]) for n in range(4)]

        mask_landed = [sem(f"mask_landed{n}") for n in range(2 * BG)]
        piece_landed = [sem(f"piece_landed{n}") for n in range(len(PIECES))]
        x_landed = [sem("x_landed0"), sem("x_landed1")]
        w_landed = sem("w_landed")
        small_landed = sem("small_landed")
        cw_landed = sem("cw_landed")
        ident_zero = sem("ident_zero")
        ident_ready = sem("ident_ready")
        kq_ready = sem("kq_ready")
        ones_ready = sem("ones_ready")
        setup_step = sem("setup_step")
        tables_ready = sem("tables_ready")
        bias_ready = sem("bias_ready")
        wT_done = sem("wT_done")
        wT_act = sem("wT_act")
        wT_dve = sem("wT_dve")
        xT_done = sem("xT_done")
        xT_ready = sem("xT_ready")
        xsT_ready = sem("xsT_ready")
        signs_act = sem("signs_act")
        signs_dve = sem("signs_dve")
        xb_ready = sem("xb_ready")
        sel_ready = sem("sel_ready")
        pick_done = sem("pick_done")
        bd_ready = sem("bd_ready")
        acc_done = sem("acc_done")
        x1_ready = sem("x1_ready")
        mix_done = sem("mix_done")
        y_ready = sem("y_ready")
        stored = sem("stored")

        block = ctx.enter_context(nc.Block())

        def piece(t, slots, lo, w):
            return t[:, slots, :, lo:lo + w]

        @block.sync
        def _(sp):
            def load_x(g, k):
                sp.dma_start(x_in[:, k, :], x_v[g, :, :]).then_inc(x_landed[k], 16)

            def load_mask(g, k, b):
                sp.dma_start(raw[:, BG * k + b, :, :], mask_v[BG * g + b, :, :, :])\
                  .then_inc(mask_landed[BG * k + b], 16)

            def free_x(g):
                sp.wait_ge(xT_done, g + 1)
                sp.wait_ge(xb_ready, g + 1)

            def free_slot(g, b):
                if b in ACT_B:
                    sp.wait_ge(signs_act, g * len(ACT_B) + ACT_B.index(b) + 1)
                else:
                    sp.wait_ge(signs_dve, g * len(DVE_B) + DVE_B.index(b) + 1)

            def store(g):
                sp.wait_ge(y_ready, g + 1)
                sp.dma_start(out_v[g, :, :], y[:, :]).then_inc(stored, 16)

            for g in range(2):
                load_x(g, g)
                for b in range(BG):
                    load_mask(g, g, b)

            def step(h, k):
                g = 2 * h + k
                free_x(g)
                load_x(g + 2, k)
                for b in range(BG):
                    free_slot(g, b)
                    load_mask(g + 2, k, b)
                store(g)

            with sp.Fori(0, (LAST - 3) // 2) as h:
                for k in range(2):
                    step(h, k)
            step((LAST - 3) // 2, 0)
            free_x(LAST - 2)
            load_x(LAST, 1)
            for n, (lo, w) in enumerate(PIECES):
                for b in range(BG):
                    if n == 0:
                        free_slot(LAST - 2, b)
                    sp.dma_start(raw[:, BG + b, :, lo:lo + w], mask_v[BG * LAST + b, :, :, lo:lo + w])\
                      .then_inc(piece_landed[n], 16)
            store(LAST - 2)
            store(LAST - 1)
            for n, (lo, w) in enumerate(PIECES):
                sp.wait_ge(y_ready, LAST + n + 1)
                sp.dma_start(out_v[LAST, :, lo:lo + w], y[:, lo:lo + w]).then_inc(stored, 16)
            sp.wait_ge(stored, 16 * (1 + LAST + len(PIECES)))

        @block.gpsimd
        def _(pool):
            nc.gpsimd.memset(ident[:, :], 0.0).then_inc(ident_zero, 1)
            pool.wait_ge(ident_zero, 1)
            nc.gpsimd.affine_select(out=ident[:, :], in_=ident[:, :], compare_op=ALU.not_equal, fill=1.0,
                                    base=0, pattern=[[-1, P]], channel_multiplier=1).then_inc(ident_ready, 1)
            pool.wait_ge(tables_ready, 1)
            pool.wait_ge(bias_ready, 1)

            def step(h, k):
                g = 2 * h + k
                pool.wait_ge(pick_done, g + 1)
                nc.gpsimd.tensor_tensor(
                    sel[:, :, :].rearrange("p j (b c) -> p j b c", b=BG),
                    ident_c[:, :].unsqueeze(1).unsqueeze(1).to_broadcast([P, J, BG, C]),
                    hit[:, :, bass.ds(BG * g, BG)].unsqueeze(3).to_broadcast([P, J, BG, C]),
                    ALU.mult).then_inc(sel_ready, 1)
                pool.wait_ge(x_landed[k], 16 * h + 16)
                pool.wait_ge(x1_ready, g + 1)
                nc.gpsimd.tensor_tensor(xb[:, :], x_in[:, k, :], bias_all[:, :], ALU.add)\
                    .then_inc(xb_ready, 1)

            with pool.Fori(0, G // 2) as h:
                for k in range(2):
                    step(h, k)

        @block.scalar
        def _(act):
            act.dma_start(w_in[:, :, :], w_v).then_inc(w_landed, 16)
            act.dma_start(cond_all[:, :], cond.unsqueeze(0).to_broadcast([P, B])).then_inc(small_landed, 16)
            act.dma_start(coeff_all[:, :], coeff.unsqueeze(0).to_broadcast([P, B])).then_inc(small_landed, 16)
            act.dma_start(bias_row[:, :], bias.unsqueeze(0)).then_inc(small_landed, 16)
            act.dma_start(cw[:, :, :], cw_v).then_inc(cw_landed, 16)
            for t in range(0, T, 2):
                act.wait_ge(wT_done, t + 1)
                nc.scalar.activation(wT[:, t, :], side[t][:, :], ACT.Copy).then_inc(wT_act, 1)

            def copy_xT(h, k):
                act.wait_ge(xT_done, 2 * h + k + 1)
                nc.scalar.activation(xT[:, k, :, :], trp[:, :, :], ACT.Copy).then_inc(xT_ready, 1)

            def step(h, k):
                for b in ACT_B:
                    act.wait_ge(mask_landed[BG * k + b], 16 * h + 16)
                    nc.scalar.activation(sgn[:, BG * k + b, :, :], raw[:, BG * k + b, :, :], ACT.Copy,
                                         bias=-1.0, scale=2.0).then_inc(signs_act, 1)
                copy_xT(h + k, 1 - k)

            copy_xT(0, 0)
            with act.Fori(0, (LAST - 1) // 2) as h:
                for k in range(2):
                    step(h, k)
            step((LAST - 1) // 2, 0)
            for n, (lo, w) in enumerate(PIECES):
                act.wait_ge(piece_landed[n], 16 * BG)
                nc.scalar.activation(sgn[:, BG, :, lo:lo + w], raw[:, BG, :, lo:lo + w], ACT.Copy,
                                     bias=-1.0, scale=2.0).then_inc(signs_act, 1)

        @block.vector
        def _(dve):
            nc.vector.nop().then_inc(x1_ready, 1)
            nc.vector.nop().then_inc(stored, 16)
            nc.vector.memset(ones[:, :], 1.0).then_inc(ones_ready, 1)
            for q in range(CJ):
                nc.vector.memset(kq[C * q:C * q + C, :], float(q)).then_inc(kq_ready, 1)
            dve.wait_ge(ident_ready, 1)
            nc.vector.tensor_reduce(ident_c[:, :], ident[:, :].rearrange("p (k c) -> p c k", c=C),
                                    AX_X, ALU.add).then_inc(setup_step, 1)
            nc.vector.tensor_reduce(blocks[:, :], ident[:, :].rearrange("p (k c) -> p k c", c=C),
                                    AX_X, ALU.add).then_inc(setup_step, 1)
            dve.wait_ge(small_landed, 48)
            nc.vector.tensor_scalar(wrap[:, :], cond_all[:, :], 0.0, float(NCOND), ALU.is_lt, ALU.mult)\
                .then_inc(setup_step, 1)
            dve.wait_ge(setup_step, 3)
            nc.vector.tensor_tensor(wrap[:, :], cond_all[:, :], wrap[:, :], ALU.add).then_inc(setup_step, 1)
            dve.wait_ge(setup_step, 4)
            nc.vector.tensor_scalar(cond_f[:, :], wrap[:, :], 0.0, float(NCOND - 1), ALU.max, ALU.min)\
                .then_inc(setup_step, 1)
            dve.wait_ge(setup_step, 5)
            dve.wait_ge(kq_ready, CJ)
            for j in range(J):
                nc.vector.tensor_scalar(hit[:, j, :], cond_f[:, :], kq[:, 0:1], float(CJ * j),
                                        ALU.subtract, ALU.is_equal).then_inc(setup_step, 1)
            dve.wait_ge(setup_step, 5 + J)
            dve.wait_ge(pick_done, 1)
            nc.vector.tensor_copy(bias_all[:, :], pick[:, :]).then_inc(bias_ready, 1)
            nc.vector.nop().then_inc(tables_ready, 1)
            for t in range(1, T, 2):
                dve.wait_ge(wT_done, t + 1)
                nc.vector.tensor_copy(wT[:, t, :], side[t][:, :]).then_inc(wT_dve, 1)

            def scale_xT(h, k):
                g = 2 * h + k
                dve.wait_ge(xT_ready, g + 1)
                nc.vector.tensor_tensor(
                    xsT[:, k, :, :].rearrange("p t (b s) -> p t b s", b=BG),
                    xT[:, k, :, :].rearrange("p t (b s) -> p t b s", b=BG),
                    coeff_all[:, bass.ds(BG * g, BG)].unsqueeze(1).unsqueeze(3).to_broadcast([P, T, BG, S]),
                    ALU.mult).then_inc(xsT_ready, 1)

            def build_bd(g):
                dve.wait_ge(pick_done, g + 2)
                nc.vector.tensor_tensor(
                    bd[:, :].rearrange("p (b d) -> p b d", b=BG),
                    pick[:, 0:C].unsqueeze(1).to_broadcast([P, BG, C]),
                    blocks[:, :].unsqueeze(2).to_broadcast([P, BG, C]),
                    ALU.mult).then_inc(bd_ready, 1)

            def step(h, k):
                g = 2 * h + k
                for b in DVE_B:
                    dve.wait_ge(mask_landed[BG * k + b], 16 * h + 16)
                    nc.vector.tensor_scalar(sgn[:, BG * k + b, :, :], raw[:, BG * k + b, :, :], 2.0, -1.0,
                                            ALU.mult, ALU.add).then_inc(signs_dve, 1)
                build_bd(g)
                scale_xT(h + k, 1 - k)
                dve.wait_ge(xb_ready, g + 1)
                dve.wait_ge(acc_done, g + 1)
                nc.vector.tensor_tensor(x1[:, :], acc[:, :], xb[:, :], ALU.add).then_inc(x1_ready, 1)
                dve.wait_ge(mix_done, g + 1)
                dve.wait_ge(stored, 16 * g + 16)
                nc.vector.tensor_tensor(y[:, :], mix[:, :], x1[:, :], ALU.add).then_inc(y_ready, 1)

            scale_xT(0, 0)
            with dve.Fori(0, (LAST - 1) // 2) as h:
                for k in range(2):
                    step(h, k)
            step((LAST - 1) // 2, 0)
            build_bd(LAST)
            dve.wait_ge(xb_ready, G)
            dve.wait_ge(stored, 16 * LAST + 16)
            for n, (lo, w) in enumerate(PIECES):
                dve.wait_ge(piece_landed[n], 16 * BG)
                nc.vector.tensor_scalar(sgn[:, BG + 1:2 * BG, :, lo:lo + w], raw[:, BG + 1:2 * BG, :, lo:lo + w],
                                        2.0, -1.0, ALU.mult, ALU.add).then_inc(signs_dve, 1)
                dve.wait_ge(acc_done, LAST + n + 1)
                nc.vector.tensor_tensor(x1[:, lo:lo + w], side[n][:, 0:w], xb[:, lo:lo + w], ALU.add)\
                    .then_inc(x1_ready, 1)
                dve.wait_ge(mix_done, LAST + n + 1)
                nc.vector.tensor_tensor(y[:, lo:lo + w], mix[:, lo:lo + w], x1[:, lo:lo + w], ALU.add)\
                    .then_inc(y_ready, 1)

        @block.tensor
        def _(pe):
            pe.wait_ge(small_landed, 48)
            pe.wait_ge(ones_ready, 1)
            nc.tensor.matmul(pick[:, :], ones[:, :], bias_row[:, :], start=True, stop=True)\
                .then_inc(pick_done, 1)
            pe.wait_ge(ident_ready, 1)
            pe.wait_ge(w_landed, 16)
            for t in range(T):
                for q in range(T):
                    last = nc.tensor.transpose(side[t][:, q * P:q * P + P],
                                               w_in[:, q, :].rearrange("p (i t) -> p t i", t=T)[:, t, :],
                                               ident[:, :])
                last.then_inc(wT_done, 1)

            def transpose_x(h, k):
                pe.wait_ge(x_landed[k], 16 * h + 16)
                for t in range(T):
                    last = nc.tensor.transpose(trp[:, t, :],
                                               x_in[:, k, :].rearrange("p (i t) -> p t i", t=T)[:, t, :],
                                               ident[:, :])
                last.then_inc(xT_done, 1)

            def gather(g):
                pe.wait_ge(sel_ready, g + 1)
                for j in range(J):
                    last = nc.tensor.matmul(pick[:, 0:C], sel[:, j, :], cw[:, j, :],
                                            start=(j == 0), stop=(j == J - 1))
                last.then_inc(pick_done, 1)

            def linear(k, bank, lo, w):
                for t in range(T):
                    nc.tensor.matmul(bank[:, 0:w], xT[:, k, t, :], wT[:, t, lo:lo + w],
                                     start=(t == 0), stop=False)

            def signed(k, bank, lo, w):
                for t in range(T):
                    for b in range(BG):
                        last = nc.tensor.matmul(bank[S * b:S * b + S, 0:w], xsT[:, k, t, S * b:S * b + S],
                                                sgn[:, BG * k + b, t, lo:lo + w],
                                                start=False, stop=(t == T - 1))
                last.then_inc(acc_done, 1)

            def step(h, k):
                g = 2 * h + k
                pe.wait_ge(xT_ready, g + 1)
                pe.wait_ge(xsT_ready, g + 1)
                linear(k, acc, 0, D)
                transpose_x(h + k, 1 - k)
                gather(g)
                pe.wait_ge(signs_act, len(ACT_B) * (g + 1))
                pe.wait_ge(signs_dve, len(DVE_B) * (g + 1))
                signed(k, acc, 0, D)
                pe.wait_ge(bd_ready, g + 1)
                pe.wait_ge(x1_ready, g + 2)
                nc.tensor.matmul(mix[:, :], bd[:, :], x1[:, :], start=True, stop=True).then_inc(mix_done, 1)

            transpose_x(0, 0)
            pe.wait_ge(cw_landed, 16)
            pe.wait_ge(wT_act, T // 2)
            pe.wait_ge(wT_dve, T // 2)
            with pe.Fori(0, (LAST - 1) // 2) as h:
                for k in range(2):
                    step(h, k)
            step((LAST - 1) // 2, 0)
            pe.wait_ge(xT_ready, G)
            pe.wait_ge(xsT_ready, G)
            for n, (lo, w) in enumerate(PIECES):
                linear(1, side[n], lo, w)
            gather(LAST)
            pe.wait_ge(bd_ready, G)
            for n, (lo, w) in enumerate(PIECES):
                pe.wait_ge(signs_act, len(ACT_B) * LAST + n + 1)
                pe.wait_ge(signs_dve, len(DVE_B) * LAST + n + 1)
                signed(1, side[n], lo, w)
                pe.wait_ge(x1_ready, LAST + n + 2)
                nc.tensor.matmul(mix[:, lo:lo + w], bd[:, :], x1[:, lo:lo + w], start=True, stop=True)\
                    .then_inc(mix_done, 1)


_INS = ["x", "condB_coeff", "itok_B_0_15", "mask_Bx4096x4096_ik1", "L0_cond_W", "L0_cond_b", "L1_cond_weights"]


def kernel(**inputs):
    import numpy as _np
    import concourse.bacc as _bacc
    from concourse import mybir as _mybir
    from concourse.bass_utils import run_bass_kernel_spmd as _run

    nc = _bacc.Bacc("TRN2", target_bir_lowering=False, num_devices=1)
    arrays, args = {}, []
    for name in _INS:
        a = _np.ascontiguousarray(inputs[name])
        arrays[f"in_{name}_dram"] = a
        args.append(nc.dram_tensor(f"in_{name}_dram", a.shape, _mybir.dt.from_np(a.dtype), kind="ExternalInput").ap())
    out = nc.dram_tensor("out_dram", inputs["x"].shape, _mybir.dt.float32, kind="ExternalOutput").ap()
    cond_resid_kernel(nc, *args, out)
    r = _run(nc, [arrays], core_ids=[0])
    return r.results[0]["out_dram"]
```

```python
from contextlib import ExitStack

import concourse.bass as bass
from concourse import mybir

F32 = mybir.dt.float32
I32 = mybir.dt.int32
ALU = mybir.AluOpType
ACT = mybir.ActivationFunctionType
AX_X = mybir.AxisListType.X

P = 128


def cond_resid_kernel(
    nc: bass.Bass,
    x: bass.AP,
    coeff: bass.AP,
    cond: bass.AP,
    mask: bass.AP,
    W: bass.AP,
    bias: bass.AP,
    weights: bass.AP,
    out: bass.AP,
):
    B, S, D = x.shape
    NCOND, C, _ = weights.shape
    T = D // P
    BG = P // S
    G = B // BG
    CJ = P // C
    J = NCOND // CJ
    LAST = G - 1
    PIECES = [(0, D // 2), (D // 2, D // 4), (3 * D // 4, D // 4)]
    EACH = BG // 2
    assert BG == T and S == C and BG * S == P and T * P == D and G % 2 == 0 and J * CJ == NCOND

    x_v = x.rearrange("(g b) s d -> g (b s) d", b=BG)
    out_v = out.rearrange("(g b) s d -> g (b s) d", b=BG)
    mask_v = mask.rearrange("b (p t) o -> b p t o", t=T)
    last_v = mask[BG * LAST:B, :, :].rearrange("b (p t) o -> t p b o", t=T)
    w_v = W.rearrange("(q o) i -> o q i", o=P)
    cw_v = weights.rearrange("(j k) c d -> (k c) j d", j=J)

    with ExitStack() as ctx:
        def sb(name, shape, dt=F32):
            return ctx.enter_context(nc.sbuf_tensor(name, shape, dt))

        def pb(name, shape):
            return ctx.enter_context(nc.psum_tensor(name, shape, F32))

        def sem(name):
            return ctx.enter_context(nc.semaphore(name))

        raw = sb("raw", [P, 2 * BG, T, D], I32)
        sgn = sb("sgn", [P, 2 * BG, T, D])
        x_in = sb("x_in", [P, 2, D])
        xT = sb("xT", [P, 2, T, P])
        xsT = sb("xsT", [P, 2, T, P])
        xb = sb("xb", [P, 2, D])
        x1 = sb("x1", [P, D])
        y = sb("y", [P, 2, D])
        w_in = sb("w_in", [P, T, D])
        wT = sb("wT", [P, T, D])
        cw = sb("cw", [P, J, C])
        sel = sb("sel", [P, J, P])
        bd = sb("bd", [P, P])
        ident = sb("ident", [P, P])
        ident_c = sb("ident_c", [P, C])
        blocks = sb("blocks", [P, BG])
        ones = sb("ones", [1, P])
        bias_row = sb("bias_row", [1, D])
        bias_all = sb("bias_all", [P, D])
        coeff_all = sb("coeff_all", [P, B])
        cond_all = sb("cond_all", [P, B], I32)
        wrap = sb("wrap", [P, B])
        cond_f = sb("cond_f", [P, B])
        kq = sb("kq", [P, 1])
        hit = sb("hit", [P, J, B])

        acc = [pb("acc0", [P, D]), pb("acc1", [P, D])]
        trp = pb("trp", [P, T, P])
        pick = pb("pick", [P, D])
        mix = pb("mix", [P, D])
        side = [pb(f"side{n}", [P, D]) for n in range(3)]
        wtr = side + [acc[1]]

        mask_landed = [sem(f"mask_landed{n}") for n in range(2 * BG)]
        piece_landed = [[sem(f"piece_landed{n}_{t}") for t in range(T)] for n in range(len(PIECES))]
        x_landed = [sem("x_landed0"), sem("x_landed1")]
        w_landed = sem("w_landed")
        small_landed = sem("small_landed")
        cw_landed = sem("cw_landed")
        ident_zero = sem("ident_zero")
        ident_ready = sem("ident_ready")
        kq_ready = sem("kq_ready")
        ones_ready = sem("ones_ready")
        setup_step = sem("setup_step")
        tables_ready = sem("tables_ready")
        bias_ready = sem("bias_ready")
        wT_done = sem("wT_done")
        wT_act = sem("wT_act")
        wT_dve = sem("wT_dve")
        xT_done = sem("xT_done")
        xT_ready = sem("xT_ready")
        xsT_ready = sem("xsT_ready")
        signs_act = sem("signs_act")
        signs_dve = sem("signs_dve")
        xb_ready = sem("xb_ready")
        sel_ready = sem("sel_ready")
        pick_done = sem("pick_done")
        bd_ready = sem("bd_ready")
        acc_done = sem("acc_done")
        x1_ready = sem("x1_ready")
        mix_done = sem("mix_done")
        y_ready = sem("y_ready")
        stored = [sem("stored0"), sem("stored1")]
        piece_stored = sem("piece_stored")

        block = ctx.enter_context(nc.Block())

        @block.sync
        def _(sp):
            def load_x(g, k):
                sp.dma_start(x_in[:, k, :], x_v[g, :, :]).then_inc(x_landed[k], 16)

            def load_mask(g, k, b):
                sp.dma_start(raw[:, BG * k + b, :, :], mask_v[BG * g + b, :, :, :])\
                  .then_inc(mask_landed[BG * k + b], 16)

            def free_x(g):
                sp.wait_ge(xT_done, g + 1)
                sp.wait_ge(xb_ready, g + 1)

            def free_slot(g, b):
                sp.wait_ge(signs_dve if b % 2 else signs_act, EACH * g + b // 2 + 1)

            sp.dma_start(w_in[:, :, :], w_v).then_inc(w_landed, 16)
            load_x(0, 0)
            load_mask(0, 0, 0)
            load_x(1, 1)
            for b in range(1, BG):
                load_mask(0, 0, b)
            load_mask(1, 1, 0)
            free_x(0)
            load_x(2, 0)
            for b in range(1, BG):
                load_mask(1, 1, b)

            def step(h, k):
                g = 2 * h + k
                free_slot(g, 0)
                load_mask(g + 2, k, 0)
                free_x(g + 1)
                load_x(g + 3, 1 - k)
                for b in range(1, BG):
                    free_slot(g, b)
                    load_mask(g + 2, k, b)

            with sp.Fori(0, (LAST - 3) // 2) as h:
                for k in range(2):
                    step(h, k)
            step((LAST - 3) // 2, 0)
            for b in range(BG):
                free_slot(LAST - 2, b)
            for n, (lo, w) in enumerate(PIECES):
                for t in range(T):
                    sp.dma_start(raw[:, BG:2 * BG, t, lo:lo + w], last_v[t, :, :, lo:lo + w])\
                      .then_inc(piece_landed[n][t], 16)
            sp.wait_ge(y_ready, LAST)
            sp.dma_start(out_v[LAST - 1, :, :], y[:, 0, :]).then_inc(stored[0], 16)
            for n, (lo, w) in enumerate(PIECES):
                sp.wait_ge(y_ready, LAST + n + 1)
                sp.dma_start(out_v[LAST, :, lo:lo + w], y[:, 1, lo:lo + w]).then_inc(piece_stored, 16)
            sp.wait_ge(piece_stored, 16 * len(PIECES))
            sp.wait_ge(stored[0], 16 * (G // 2 + 1))
            sp.wait_ge(stored[1], 16 * (G // 2))

        @block.gpsimd
        def _(pool):
            nc.gpsimd.memset(ident[:, :], 0.0).then_inc(ident_zero, 1)
            pool.wait_ge(ident_zero, 1)
            nc.gpsimd.affine_select(out=ident[:, :], in_=ident[:, :], compare_op=ALU.not_equal, fill=1.0,
                                    base=0, pattern=[[-1, P]], channel_multiplier=1).then_inc(ident_ready, 1)
            pool.wait_ge(tables_ready, 1)
            pool.wait_ge(bias_ready, 1)

            def select(g):
                pool.wait_ge(pick_done, g + 1)
                nc.gpsimd.tensor_tensor(
                    sel[:, :, :].rearrange("p j (b c) -> p j b c", b=BG),
                    ident_c[:, :].unsqueeze(1).unsqueeze(1).to_broadcast([P, J, BG, C]),
                    hit[:, :, bass.ds(BG * g, BG)].unsqueeze(3).to_broadcast([P, J, BG, C]),
                    ALU.mult).then_inc(sel_ready, 1)

            def add_bias(h, k):
                pool.wait_ge(x_landed[k], 16 * h + 16)
                pool.wait_ge(x1_ready, 2 * h + k + 1)
                nc.gpsimd.tensor_tensor(xb[:, k, :], x_in[:, k, :], bias_all[:, :], ALU.add)\
                    .then_inc(xb_ready, 1)

            with pool.Fori(0, G // 2) as h:
                for k in range(2):
                    select(2 * h + k)
                    add_bias(h, k)

        @block.scalar
        def _(act):
            act.dma_start(bias_row[:, :], bias.unsqueeze(0)).then_inc(small_landed, 16)
            act.dma_start(cond_all[:, :], cond.unsqueeze(0).to_broadcast([P, B])).then_inc(small_landed, 16)
            act.dma_start(coeff_all[:, :], coeff.unsqueeze(0).to_broadcast([P, B])).then_inc(small_landed, 16)
            act.dma_start(cw[:, :, :], cw_v).then_inc(cw_landed, 16)
            for t in range(0, T, 2):
                act.wait_ge(wT_done, t + 1)
                nc.scalar.activation(wT[:, t, :], wtr[t][:, :], ACT.Copy).then_inc(wT_act, 1)

            def copy_xT(h, k):
                act.wait_ge(xT_done, 2 * h + k + 1)
                nc.scalar.activation(xT[:, k, :, :], trp[:, :, :], ACT.Copy).then_inc(xT_ready, 1)

            def convert(h, k, b):
                act.wait_ge(mask_landed[BG * k + b], 16 * h + 16)
                nc.scalar.activation(sgn[:, BG * k + b, :, :], raw[:, BG * k + b, :, :], ACT.Copy,
                                     bias=-1.0, scale=2.0).then_inc(signs_act, 1)

            def step(h, k):
                g = 2 * h + k
                convert(h + k, 1 - k, 0)
                copy_xT(h + 1, k)
                act.wait_ge(y_ready, g + 1)
                act.dma_start(out_v[g, :, :], y[:, k, :]).then_inc(stored[k], 16)
                convert(h + k, 1 - k, 2)

            copy_xT(0, 0)
            convert(0, 0, 0)
            copy_xT(0, 1)
            convert(0, 0, 2)
            with act.Fori(0, (LAST - 1) // 2) as h:
                for k in range(2):
                    step(h, k)
            for n, (lo, w) in enumerate(PIECES):
                for t in range(0, T, 2):
                    act.wait_ge(piece_landed[n][t], 16)
                    nc.scalar.activation(sgn[:, BG:2 * BG, t, lo:lo + w], raw[:, BG:2 * BG, t, lo:lo + w],
                                         ACT.Copy, bias=-1.0, scale=2.0).then_inc(signs_act, 1)

        @block.vector
        def _(dve):
            nc.vector.nop().then_inc(x1_ready, 2)
            for k in range(2):
                nc.vector.nop().then_inc(stored[k], 16)
            nc.vector.memset(ones[:, :], 1.0).then_inc(ones_ready, 1)
            for q in range(CJ):
                nc.vector.memset(kq[C * q:C * q + C, :], float(q)).then_inc(kq_ready, 1)
            dve.wait_ge(ident_ready, 1)
            nc.vector.tensor_reduce(ident_c[:, :], ident[:, :].rearrange("p (k c) -> p c k", c=C),
                                    AX_X, ALU.add).then_inc(setup_step, 1)
            nc.vector.tensor_reduce(blocks[:, :], ident[:, :].rearrange("p (k c) -> p k c", c=C),
                                    AX_X, ALU.add).then_inc(setup_step, 1)
            dve.wait_ge(small_landed, 48)
            nc.vector.tensor_scalar(wrap[:, :], cond_all[:, :], 0.0, float(NCOND), ALU.is_lt, ALU.mult)\
                .then_inc(setup_step, 1)
            dve.wait_ge(setup_step, 3)
            nc.vector.tensor_tensor(wrap[:, :], cond_all[:, :], wrap[:, :], ALU.add).then_inc(setup_step, 1)
            dve.wait_ge(setup_step, 4)
            nc.vector.tensor_scalar(cond_f[:, :], wrap[:, :], 0.0, float(NCOND - 1), ALU.max, ALU.min)\
                .then_inc(setup_step, 1)
            dve.wait_ge(setup_step, 5)
            dve.wait_ge(kq_ready, CJ)
            for j in range(J):
                nc.vector.tensor_scalar(hit[:, j, :], cond_f[:, :], kq[:, 0:1], float(CJ * j),
                                        ALU.subtract, ALU.is_equal).then_inc(setup_step, 1)
            dve.wait_ge(setup_step, 5 + J)
            dve.wait_ge(pick_done, 1)
            nc.vector.tensor_copy(bias_all[:, :], pick[:, :]).then_inc(bias_ready, 1)
            nc.vector.nop().then_inc(tables_ready, 1)
            for t in range(1, T, 2):
                dve.wait_ge(wT_done, t + 1)
                nc.vector.tensor_copy(wT[:, t, :], wtr[t][:, :]).then_inc(wT_dve, 1)

            def scale_xT(h, k):
                g = 2 * h + k
                dve.wait_ge(xT_ready, g + 1)
                nc.vector.tensor_tensor(
                    xsT[:, k, :, :].rearrange("p t (b s) -> p t b s", b=BG),
                    xT[:, k, :, :].rearrange("p t (b s) -> p t b s", b=BG),
                    coeff_all[:, bass.ds(BG * g, BG)].unsqueeze(1).unsqueeze(3).to_broadcast([P, T, BG, S]),
                    ALU.mult).then_inc(xsT_ready, 1)

            def build_bd(g):
                dve.wait_ge(pick_done, g + 2)
                nc.vector.tensor_tensor(
                    bd[:, :].rearrange("p (b d) -> p b d", b=BG),
                    pick[:, 0:C].unsqueeze(1).to_broadcast([P, BG, C]),
                    blocks[:, :].unsqueeze(2).to_broadcast([P, BG, C]),
                    ALU.mult).then_inc(bd_ready, 1)

            def convert(h, k, b):
                dve.wait_ge(mask_landed[BG * k + b], 16 * h + 16)
                nc.vector.tensor_scalar(sgn[:, BG * k + b, :, :], raw[:, BG * k + b, :, :], 2.0, -1.0,
                                        ALU.mult, ALU.add).then_inc(signs_dve, 1)

            def convert_piece(n, t):
                lo, w = PIECES[n]
                dve.wait_ge(piece_landed[n][t], 16)
                nc.vector.tensor_scalar(sgn[:, BG:2 * BG, t, lo:lo + w], raw[:, BG:2 * BG, t, lo:lo + w],
                                        2.0, -1.0, ALU.mult, ALU.add).then_inc(signs_dve, 1)

            def add_x1(n, k, bank, lo, w):
                dve.wait_ge(acc_done, n + 1)
                nc.vector.tensor_tensor(x1[:, lo:lo + w], bank[:, 0:w], xb[:, k, lo:lo + w], ALU.add)\
                    .then_inc(x1_ready, 1)

            def add_y(n, k, lo, w):
                dve.wait_ge(mix_done, n + 1)
                nc.vector.tensor_tensor(y[:, k, lo:lo + w], mix[:, lo:lo + w], x1[:, lo:lo + w], ALU.add)\
                    .then_inc(y_ready, 1)

            def step(h, k):
                g = 2 * h + k
                convert(h, k, 3)
                scale_xT(h + k, 1 - k)
                dve.wait_ge(xb_ready, g + 1)
                add_x1(g, k, acc[k], 0, D)
                convert(h + k, 1 - k, 1)
                dve.wait_ge(stored[k], 16 * h + 16)
                add_y(g, k, 0, D)
                build_bd(g + 1)

            scale_xT(0, 0)
            build_bd(0)
            convert(0, 0, 1)
            with dve.Fori(0, (LAST - 1) // 2) as h:
                for k in range(2):
                    step(h, k)
            convert((LAST - 1) // 2, 0, 3)
            scale_xT((LAST - 1) // 2, 1)
            convert_piece(0, 1)
            dve.wait_ge(xb_ready, LAST)
            add_x1(LAST - 1, 0, acc[0], 0, D)
            convert_piece(0, 3)
            dve.wait_ge(stored[0], 16 * (G // 2))
            add_y(LAST - 1, 0, 0, D)
            build_bd(LAST)
            dve.wait_ge(xb_ready, G)
            dve.wait_ge(y_ready, LAST)
            for n, (lo, w) in enumerate(PIECES):
                if n + 1 < len(PIECES):
                    convert_piece(n + 1, 1)
                add_x1(LAST + n, 1, side[n], lo, w)
                if n + 1 < len(PIECES):
                    convert_piece(n + 1, 3)
                if n == 0:
                    dve.wait_ge(stored[1], 16 * (G // 2))
                add_y(LAST + n, 1, lo, w)

        @block.tensor
        def _(pe):
            pe.wait_ge(small_landed, 48)
            pe.wait_ge(ones_ready, 1)
            nc.tensor.matmul(pick[:, :], ones[:, :], bias_row[:, :], start=True, stop=True)\
                .then_inc(pick_done, 1)
            pe.wait_ge(ident_ready, 1)
            pe.wait_ge(w_landed, 16)
            for t in range(T):
                for q in range(D // P):
                    last = nc.tensor.transpose(wtr[t][:, q * P:q * P + P],
                                               w_in[:, q, :].rearrange("p (i t) -> p t i", t=T)[:, t, :],
                                               ident[:, :])
                last.then_inc(wT_done, 1)

            def transpose_x(h, k):
                pe.wait_ge(x_landed[k], 16 * h + 16)
                for t in range(T):
                    last = nc.tensor.transpose(trp[:, t, :],
                                               x_in[:, k, :].rearrange("p (i t) -> p t i", t=T)[:, t, :],
                                               ident[:, :])
                last.then_inc(xT_done, 1)

            def gather(g):
                pe.wait_ge(sel_ready, g + 1)
                for j in range(J):
                    last = nc.tensor.matmul(pick[:, 0:C], sel[:, j, :], cw[:, j, :],
                                            start=(j == 0), stop=(j == J - 1))
                last.then_inc(pick_done, 1)

            def linear(k, bank, lo, w):
                for t in range(T):
                    nc.tensor.matmul(bank[:, 0:w], xT[:, k, t, :], wT[:, t, lo:lo + w],
                                     start=(t == 0), stop=False)

            def signed(k, bank, n, t, lo, w):
                for b in range(BG):
                    last = nc.tensor.matmul(bank[S * b:S * b + S, 0:w], xsT[:, k, t, S * b:S * b + S],
                                            sgn[:, BG * k + b, t, lo:lo + w],
                                            start=False, stop=(t == T - 1))
                if t == T - 1:
                    last.then_inc(acc_done, 1)

            def second(n, lo, w):
                pe.wait_ge(x1_ready, n + 3)
                nc.tensor.matmul(mix[:, lo:lo + w], bd[:, :], x1[:, lo:lo + w], start=True, stop=True)\
                    .then_inc(mix_done, 1)

            def step(h, k):
                g = 2 * h + k
                pe.wait_ge(xT_ready, g + 2)
                linear(1 - k, acc[1 - k], 0, D)
                pe.wait_ge(bd_ready, g + 1)
                gather(g + 1)
                pe.wait_ge(xsT_ready, g + 1)
                pe.wait_ge(signs_act, EACH * (g + 1))
                pe.wait_ge(signs_dve, EACH * (g + 1))
                for t in range(T):
                    signed(k, acc[k], g, t, 0, D)
                transpose_x(h + 1, k)
                second(g, 0, D)

            transpose_x(0, 0)
            pe.wait_ge(cw_landed, 16)
            pe.wait_ge(wT_act, T // 2)
            pe.wait_ge(wT_dve, T // 2)
            pe.wait_ge(xT_ready, 1)
            linear(0, acc[0], 0, D)
            transpose_x(0, 1)
            pe.wait_ge(bias_ready, 1)
            gather(0)
            with pe.Fori(0, (LAST - 1) // 2) as h:
                for k in range(2):
                    step(h, k)
            pe.wait_ge(xT_ready, G)
            for n, (lo, w) in enumerate(PIECES):
                linear(1, side[n], lo, w)
            pe.wait_ge(bd_ready, LAST)
            gather(LAST)
            pe.wait_ge(xsT_ready, LAST)
            pe.wait_ge(signs_act, EACH * LAST)
            pe.wait_ge(signs_dve, EACH * LAST)
            for t in range(T):
                signed(0, acc[0], LAST - 1, t, 0, D)
            second(LAST - 1, 0, D)
            pe.wait_ge(xsT_ready, G)
            for n, (lo, w) in enumerate(PIECES):
                for t in range(T):
                    pe.wait_ge(signs_dve if t % 2 else signs_act, EACH * (LAST + n) + t // 2 + 1)
                    signed(1, side[n], LAST + n, t, lo, w)
                if n == 0:
                    pe.wait_ge(bd_ready, G)
                second(LAST + n, lo, w)


_INS = ["x", "condB_coeff", "itok_B_0_15", "mask_Bx4096x4096_ik1", "L0_cond_W", "L0_cond_b", "L1_cond_weights"]


def kernel(**inputs):
    import numpy as _np
    import concourse.bacc as _bacc
    from concourse import mybir as _mybir
    from concourse.bass_utils import run_bass_kernel_spmd as _run

    nc = _bacc.Bacc("TRN2", target_bir_lowering=False, num_devices=1)
    arrays, args = {}, []
    for name in _INS:
        a = _np.ascontiguousarray(inputs[name])
        arrays[f"in_{name}_dram"] = a
        args.append(nc.dram_tensor(f"in_{name}_dram", a.shape, _mybir.dt.from_np(a.dtype), kind="ExternalInput").ap())
    out = nc.dram_tensor("out_dram", inputs["x"].shape, _mybir.dt.float32, kind="ExternalOutput").ap()
    cond_resid_kernel(nc, *args, out)
    r = _run(nc, [arrays], core_ids=[0])
    return r.results[0]["out_dram"]
```

```python
from contextlib import ExitStack

import concourse.bass as bass
from concourse import mybir

F32 = mybir.dt.float32
I32 = mybir.dt.int32
ALU = mybir.AluOpType
ACT = mybir.ActivationFunctionType
AX_X = mybir.AxisListType.X

P = 128


def cond_resid_kernel(
    nc: bass.Bass,
    x: bass.AP,
    coeff: bass.AP,
    cond: bass.AP,
    mask: bass.AP,
    W: bass.AP,
    bias: bass.AP,
    weights: bass.AP,
    out: bass.AP,
):
    B, S, D = x.shape
    NCOND, C, _ = weights.shape
    T = D // P
    BG = P // S
    G = B // BG
    CJ = P // C
    J = NCOND // CJ
    LAST = G - 1
    PIECES = [(0, D // 2), (D // 2, D // 4), (3 * D // 4, D // 4)]
    EACH = T // 2
    assert S == C and BG * S == P and T * P == D and G % 2 == 0 and J * CJ == NCOND

    x_v = x.rearrange("(g b) s d -> g (b s) d", b=BG)
    out_v = out.rearrange("(g b) s d -> g (b s) d", b=BG)
    mask_v = mask.rearrange("(g b) (t p) o -> g t p b o", b=BG, p=P)
    w_v = W.rearrange("(q o) i -> o q i", o=P)
    cw_v = weights.rearrange("(j k) c d -> (k c) j d", j=J)

    with ExitStack() as ctx:
        def sb(name, shape, dt=F32):
            return ctx.enter_context(nc.sbuf_tensor(name, shape, dt))

        def pb(name, shape):
            return ctx.enter_context(nc.psum_tensor(name, shape, F32))

        def sem(name):
            return ctx.enter_context(nc.semaphore(name))

        raw = sb("raw", [P, 2 * T, BG, D], I32)
        sgn = sb("sgn", [P, 2 * T, BG, D])
        x_in = sb("x_in", [P, 2, D])
        xT = sb("xT", [P, 2, T, P])
        xsT = sb("xsT", [P, 2, T, P])
        xb = sb("xb", [P, 2, D])
        x1 = sb("x1", [P, D])
        y = sb("y", [P, 2, D])
        y_last = sb("y_last", [P, D])
        w_in = sb("w_in", [P, T, D])
        wT = sb("wT", [P, T, D])
        cw = sb("cw", [P, J, C])
        sel = sb("sel", [P, J, P])
        bd = sb("bd", [P, P])
        ident = sb("ident", [P, P])
        ident_c = sb("ident_c", [P, C])
        blocks = sb("blocks", [P, BG])
        ones = sb("ones", [1, P])
        bias_row = sb("bias_row", [1, D])
        bias_all = sb("bias_all", [P, D])
        coeff_all = sb("coeff_all", [P, B])
        cond_all = sb("cond_all", [P, B], I32)
        wrap = sb("wrap", [P, B])
        cond_f = sb("cond_f", [P, B])
        kq = sb("kq", [P, 1])
        hit = sb("hit", [P, J, B])

        acc = [pb("acc0", [P, D]), pb("acc1", [P, D])]
        trp = pb("trp", [P, T, P])
        pick = pb("pick", [P, D])
        mix = pb("mix", [P, D])
        side = [pb(f"side{n}", [P, D]) for n in range(len(PIECES))]
        wtr = side + [acc[1]]

        mask_landed = [sem(f"mask_landed{n}") for n in range(2 * T)]
        piece_landed = [[sem(f"piece_landed{n}_{t}") for t in range(T)] for n in range(len(PIECES))]
        x_landed = [sem("x_landed0"), sem("x_landed1")]
        w_landed = sem("w_landed")
        small_landed = sem("small_landed")
        cw_landed = sem("cw_landed")
        ident_zero = sem("ident_zero")
        ident_ready = sem("ident_ready")
        kq_ready = sem("kq_ready")
        ones_ready = sem("ones_ready")
        setup_step = sem("setup_step")
        tables_ready = sem("tables_ready")
        bias_ready = sem("bias_ready")
        wT_done = sem("wT_done")
        wT_act = sem("wT_act")
        wT_dve = sem("wT_dve")
        xT_done = sem("xT_done")
        xT_ready = sem("xT_ready")
        xsT_ready = sem("xsT_ready")
        signs_act = sem("signs_act")
        signs_dve = sem("signs_dve")
        xb_ready = sem("xb_ready")
        sel_ready = sem("sel_ready")
        pick_done = sem("pick_done")
        bd_ready = sem("bd_ready")
        acc_done = sem("acc_done")
        x1_ready = sem("x1_ready")
        mix_done = sem("mix_done")
        y_ready = sem("y_ready")
        stored = [sem("stored0"), sem("stored1")]
        piece_stored = sem("piece_stored")
        block = ctx.enter_context(nc.Block())

        @block.sync
        def _(sp):
            def load_x(g, k):
                sp.dma_start(x_in[:, k, :], x_v[g, :, :]).then_inc(x_landed[k], 16)

            def load_mask(g, k, t):
                sp.dma_start(raw[:, T * k + t, :, :], mask_v[g, t, :, :, :]).then_inc(mask_landed[T * k + t], 16)

            def free_x(g):
                sp.wait_ge(xT_done, g + 1)
                sp.wait_ge(xb_ready, g + 1)

            def free_slot(g, t):
                sp.wait_ge(signs_dve if t % 2 else signs_act, EACH * g + t // 2 + 1)

            sp.dma_start(w_in[:, :, :], w_v).then_inc(w_landed, 16)
            load_x(0, 0)
            load_mask(0, 0, 0)
            load_x(1, 1)
            for t in range(1, T):
                load_mask(0, 0, t)
            load_mask(1, 1, 0)
            free_x(0)
            load_x(2, 0)
            for t in range(1, T):
                load_mask(1, 1, t)

            def step(h, k):
                g = 2 * h + k
                free_slot(g, 0)
                load_mask(g + 2, k, 0)
                free_x(g + 1)
                load_x(g + 3, 1 - k)
                for t in range(1, T):
                    free_slot(g, t)
                    load_mask(g + 2, k, t)

            with sp.Fori(0, (LAST - 3) // 2) as h:
                for k in range(2):
                    step(h, k)
            step((LAST - 3) // 2, 0)
            for t in range(T):
                free_slot(LAST - 2, t)
            for n, (lo, w) in enumerate(PIECES):
                for t in range(T):
                    sp.dma_start(raw[:, T + t, :, lo:lo + w], mask_v[LAST, t, :, :, lo:lo + w])\
                      .then_inc(piece_landed[n][t], 16)
            sp.wait_ge(y_ready, LAST)
            sp.dma_start(out_v[LAST - 1, :, :], y[:, 0, :]).then_inc(stored[0], 16)
            for n, (lo, w) in enumerate(PIECES):
                sp.wait_ge(y_ready, LAST + n + 1)
                sp.dma_start(out_v[LAST, :, lo:lo + w], y_last[:, lo:lo + w]).then_inc(piece_stored, 16)
            sp.wait_ge(piece_stored, 16 * len(PIECES))
            sp.wait_ge(stored[0], 16 * (G // 2 + 1))
            sp.wait_ge(stored[1], 16 * (G // 2))

        @block.gpsimd
        def _(pool):
            nc.gpsimd.memset(ident[:, :], 0.0).then_inc(ident_zero, 1)
            pool.wait_ge(ident_zero, 1)
            nc.gpsimd.affine_select(out=ident[:, :], in_=ident[:, :], compare_op=ALU.not_equal, fill=1.0,
                                    base=0, pattern=[[-1, P]], channel_multiplier=1).then_inc(ident_ready, 1)
            pool.wait_ge(tables_ready, 1)
            pool.wait_ge(bias_ready, 1)

            def select(g):
                pool.wait_ge(pick_done, g + 1)
                nc.gpsimd.tensor_tensor(
                    sel[:, :, :].rearrange("p j (b c) -> p j b c", b=BG),
                    ident_c[:, :].unsqueeze(1).unsqueeze(1).to_broadcast([P, J, BG, C]),
                    hit[:, :, bass.ds(BG * g, BG)].unsqueeze(3).to_broadcast([P, J, BG, C]),
                    ALU.mult).then_inc(sel_ready, 1)

            def add_bias(h, k):
                pool.wait_ge(x_landed[k], 16 * h + 16)
                pool.wait_ge(x1_ready, 2 * h + k + 1)
                nc.gpsimd.tensor_tensor(xb[:, k, :], x_in[:, k, :], bias_all[:, :], ALU.add)\
                    .then_inc(xb_ready, 1)

            with pool.Fori(0, G // 2) as h:
                for k in range(2):
                    select(2 * h + k)
                    add_bias(h, k)

        @block.scalar
        def _(act):
            act.dma_start(bias_row[:, :], bias.unsqueeze(0)).then_inc(small_landed, 16)
            act.dma_start(cond_all[:, :], cond.unsqueeze(0).to_broadcast([P, B])).then_inc(small_landed, 16)
            act.dma_start(coeff_all[:, :], coeff.unsqueeze(0).to_broadcast([P, B])).then_inc(small_landed, 16)
            act.dma_start(cw[:, :, :], cw_v).then_inc(cw_landed, 16)
            for t in range(0, T, 2):
                act.wait_ge(wT_done, t + 1)
                nc.scalar.activation(wT[:, t, :], wtr[t][:, :], ACT.Copy).then_inc(wT_act, 1)

            def copy_xT(h, k):
                act.wait_ge(xT_done, 2 * h + k + 1)
                nc.scalar.activation(xT[:, k, :, :], trp[:, :, :], ACT.Copy).then_inc(xT_ready, 1)

            def convert(h, k, t):
                act.wait_ge(mask_landed[T * k + t], 16 * h + 16)
                nc.scalar.activation(sgn[:, T * k + t, :, :], raw[:, T * k + t, :, :], ACT.Copy,
                                     bias=-1.0, scale=2.0).then_inc(signs_act, 1)

            def step(h, k):
                g = 2 * h + k
                convert(h, k, 2)
                convert(h + k, 1 - k, 0)
                copy_xT(h + 1, k)
                act.wait_ge(y_ready, g + 1)
                act.dma_start(out_v[g, :, :], y[:, k, :]).then_inc(stored[k], 16)

            copy_xT(0, 0)
            copy_xT(0, 1)
            convert(0, 0, 0)
            with act.Fori(0, (LAST - 1) // 2) as h:
                for k in range(2):
                    step(h, k)
            convert((LAST - 1) // 2, 0, 2)
            for n, (lo, w) in enumerate(PIECES):
                for t in range(0, T, 2):
                    act.wait_ge(piece_landed[n][t], 16)
                    nc.scalar.activation(sgn[:, T + t, :, lo:lo + w], raw[:, T + t, :, lo:lo + w],
                                         ACT.Copy, bias=-1.0, scale=2.0).then_inc(signs_act, 1)

        @block.vector
        def _(dve):
            nc.vector.nop().then_inc(x1_ready, 2)
            for k in range(2):
                nc.vector.nop().then_inc(stored[k], 16)
            nc.vector.memset(ones[:, :], 1.0).then_inc(ones_ready, 1)
            for q in range(CJ):
                nc.vector.memset(kq[C * q:C * q + C, :], float(q)).then_inc(kq_ready, 1)
            dve.wait_ge(ident_ready, 1)
            nc.vector.tensor_reduce(ident_c[:, :], ident[:, :].rearrange("p (k c) -> p c k", c=C),
                                    AX_X, ALU.add).then_inc(setup_step, 1)
            nc.vector.tensor_reduce(blocks[:, :], ident[:, :].rearrange("p (k c) -> p k c", c=C),
                                    AX_X, ALU.add).then_inc(setup_step, 1)
            dve.wait_ge(small_landed, 48)
            nc.vector.tensor_scalar(wrap[:, :], cond_all[:, :], 0.0, float(NCOND), ALU.is_lt, ALU.mult)\
                .then_inc(setup_step, 1)
            dve.wait_ge(setup_step, 3)
            nc.vector.tensor_tensor(wrap[:, :], cond_all[:, :], wrap[:, :], ALU.add).then_inc(setup_step, 1)
            dve.wait_ge(setup_step, 4)
            nc.vector.tensor_scalar(cond_f[:, :], wrap[:, :], 0.0, float(NCOND - 1), ALU.max, ALU.min)\
                .then_inc(setup_step, 1)
            dve.wait_ge(setup_step, 5)
            dve.wait_ge(kq_ready, CJ)
            for j in range(J):
                nc.vector.tensor_scalar(hit[:, j, :], cond_f[:, :], kq[:, 0:1], float(CJ * j),
                                        ALU.subtract, ALU.is_equal).then_inc(setup_step, 1)
            dve.wait_ge(setup_step, 5 + J)
            dve.wait_ge(pick_done, 1)
            nc.vector.tensor_copy(bias_all[:, :], pick[:, :]).then_inc(bias_ready, 1)
            nc.vector.nop().then_inc(tables_ready, 1)
            for t in range(1, T, 2):
                dve.wait_ge(wT_done, t + 1)
                nc.vector.tensor_copy(wT[:, t, :], wtr[t][:, :]).then_inc(wT_dve, 1)

            def scale_xT(h, k):
                g = 2 * h + k
                dve.wait_ge(xT_ready, g + 1)
                nc.vector.tensor_tensor(
                    xsT[:, k, :, :].rearrange("p t (b s) -> p t b s", b=BG),
                    xT[:, k, :, :].rearrange("p t (b s) -> p t b s", b=BG),
                    coeff_all[:, bass.ds(BG * g, BG)].unsqueeze(1).unsqueeze(3).to_broadcast([P, T, BG, S]),
                    ALU.mult).then_inc(xsT_ready, 1)

            def build_bd(g):
                dve.wait_ge(pick_done, g + 2)
                nc.vector.tensor_tensor(
                    bd[:, :].rearrange("p (b d) -> p b d", b=BG),
                    pick[:, 0:C].unsqueeze(1).to_broadcast([P, BG, C]),
                    blocks[:, :].unsqueeze(2).to_broadcast([P, BG, C]),
                    ALU.mult).then_inc(bd_ready, 1)

            def convert(h, k, t):
                dve.wait_ge(mask_landed[T * k + t], 16 * h + 16)
                nc.vector.tensor_scalar(sgn[:, T * k + t, :, :], raw[:, T * k + t, :, :], 2.0, -1.0,
                                        ALU.mult, ALU.add).then_inc(signs_dve, 1)

            def convert_piece(n, t):
                lo, w = PIECES[n]
                dve.wait_ge(piece_landed[n][t], 16)
                nc.vector.tensor_scalar(sgn[:, T + t, :, lo:lo + w], raw[:, T + t, :, lo:lo + w],
                                        2.0, -1.0, ALU.mult, ALU.add).then_inc(signs_dve, 1)

            def add_x1(n, k, bank, lo, w):
                dve.wait_ge(acc_done, n + 1)
                nc.vector.tensor_tensor(x1[:, lo:lo + w], bank[:, 0:w], xb[:, k, lo:lo + w], ALU.add)\
                    .then_inc(x1_ready, 1)

            def add_y(n, half, lo, w):
                dve.wait_ge(mix_done, n + 1)
                nc.vector.tensor_tensor(half[:, lo:lo + w], mix[:, lo:lo + w], x1[:, lo:lo + w], ALU.add)\
                    .then_inc(y_ready, 1)

            def step(h, k):
                g = 2 * h + k
                convert(h, k, 3)
                dve.wait_ge(xb_ready, g + 1)
                add_x1(g, k, acc[k], 0, D)
                convert(h + k, 1 - k, 1)
                dve.wait_ge(stored[k], 16 * h + 16)
                add_y(g, y[:, k, :], 0, D)
                build_bd(g + 1)
                scale_xT(h + 1, k)

            scale_xT(0, 0)
            build_bd(0)
            scale_xT(0, 1)
            convert(0, 0, 1)
            with dve.Fori(0, (LAST - 1) // 2) as h:
                for k in range(2):
                    step(h, k)
            convert((LAST - 1) // 2, 0, 3)
            dve.wait_ge(xb_ready, LAST)
            add_x1(LAST - 1, 0, acc[0], 0, D)
            convert_piece(0, 1)
            dve.wait_ge(stored[0], 16 * (G // 2))
            add_y(LAST - 1, y[:, 0, :], 0, D)
            build_bd(LAST)
            convert_piece(0, 3)
            dve.wait_ge(xb_ready, G)
            dve.wait_ge(y_ready, LAST)
            for n, (lo, w) in enumerate(PIECES):
                add_x1(LAST + n, 1, side[n], lo, w)
                if n + 1 < len(PIECES):
                    convert_piece(n + 1, 1)
                add_y(LAST + n, y_last, lo, w)
                if n + 1 < len(PIECES):
                    convert_piece(n + 1, 3)

        @block.tensor
        def _(pe):
            pe.wait_ge(small_landed, 48)
            pe.wait_ge(ones_ready, 1)
            nc.tensor.matmul(pick[:, :], ones[:, :], bias_row[:, :], start=True, stop=True)\
                .then_inc(pick_done, 1)
            pe.wait_ge(ident_ready, 1)
            pe.wait_ge(w_landed, 16)
            for t in range(T):
                for q in range(D // P):
                    last = nc.tensor.transpose(wtr[t][:, q * P:q * P + P],
                                               w_in[:, q, t * P:t * P + P],
                                               ident[:, :])
                last.then_inc(wT_done, 1)

            def transpose_x(h, k):
                pe.wait_ge(x_landed[k], 16 * h + 16)
                for t in range(T):
                    last = nc.tensor.transpose(trp[:, t, :],
                                               x_in[:, k, t * P:t * P + P],
                                               ident[:, :])
                last.then_inc(xT_done, 1)

            def gather(g):
                pe.wait_ge(sel_ready, g + 1)
                for j in range(J):
                    last = nc.tensor.matmul(pick[:, 0:C], sel[:, j, :], cw[:, j, :],
                                            start=(j == 0), stop=(j == J - 1))
                last.then_inc(pick_done, 1)

            def linear(k, bank, lo, w):
                for t in range(T):
                    nc.tensor.matmul(bank[:, 0:w], xT[:, k, t, :], wT[:, t, lo:lo + w],
                                     start=(t == 0), stop=False)

            def signed(g, k, bank, t, lo, w):
                pe.wait_ge(signs_dve if t % 2 else signs_act, EACH * g + t // 2 + 1)
                for b in range(BG):
                    last = nc.tensor.matmul(bank[S * b:S * b + S, 0:w], xsT[:, k, t, S * b:S * b + S],
                                            sgn[:, T * k + t, b, lo:lo + w],
                                            start=False, stop=(t == T - 1))
                if t == T - 1:
                    last.then_inc(acc_done, 1)

            def second(n, lo, w):
                pe.wait_ge(x1_ready, n + 3)
                nc.tensor.matmul(mix[:, lo:lo + w], bd[:, :], x1[:, lo:lo + w], start=True, stop=True)\
                    .then_inc(mix_done, 1)

            def step(h, k):
                g = 2 * h + k
                signed(g, k, acc[k], 1, 0, D)
                pe.wait_ge(xT_ready, g + 2)
                linear(1 - k, acc[1 - k], 0, D)
                signed(g, k, acc[k], 2, 0, D)
                pe.wait_ge(bd_ready, g + 1)
                gather(g + 1)
                signed(g, k, acc[k], 3, 0, D)
                pe.wait_ge(xsT_ready, g + 2)
                signed(g + 1, 1 - k, acc[1 - k], 0, 0, D)
                second(g, 0, D)
                transpose_x(h + 1, k)

            transpose_x(0, 0)
            pe.wait_ge(cw_landed, 16)
            pe.wait_ge(wT_act, T // 2)
            pe.wait_ge(wT_dve, T // 2)
            pe.wait_ge(xT_ready, 1)
            linear(0, acc[0], 0, D)
            transpose_x(0, 1)
            pe.wait_ge(bias_ready, 1)
            gather(0)
            pe.wait_ge(xsT_ready, 1)
            signed(0, 0, acc[0], 0, 0, D)
            with pe.Fori(0, (LAST - 1) // 2) as h:
                for k in range(2):
                    step(h, k)
            signed(LAST - 1, 0, acc[0], 1, 0, D)
            pe.wait_ge(xT_ready, G)
            for n, (lo, w) in enumerate(PIECES):
                linear(1, side[n], lo, w)
            signed(LAST - 1, 0, acc[0], 2, 0, D)
            pe.wait_ge(bd_ready, LAST)
            gather(LAST)
            signed(LAST - 1, 0, acc[0], 3, 0, D)
            pe.wait_ge(xsT_ready, G)
            for n, (lo, w) in enumerate(PIECES):
                signed(LAST + n, 1, side[n], 0, lo, w)
                if n == 0:
                    second(LAST - 1, 0, D)
                signed(LAST + n, 1, side[n], 1, lo, w)
                if n == 1:
                    pe.wait_ge(bd_ready, G)
                if n >= 1:
                    second(LAST + n - 1, *PIECES[n - 1])
                for t in range(2, T):
                    signed(LAST + n, 1, side[n], t, lo, w)
            second(LAST + len(PIECES) - 1, *PIECES[-1])


_INS = ["x", "condB_coeff", "itok_B_0_15", "mask_Bx4096x4096_ik1", "L0_cond_W", "L0_cond_b", "L1_cond_weights"]


def kernel(**inputs):
    import numpy as _np
    import concourse.bacc as _bacc
    from concourse import mybir as _mybir
    from concourse.bass_utils import run_bass_kernel_spmd as _run

    nc = _bacc.Bacc("TRN2", target_bir_lowering=False, num_devices=1)
    arrays, args = {}, []
    for name in _INS:
        a = _np.ascontiguousarray(inputs[name])
        arrays[f"in_{name}_dram"] = a
        args.append(nc.dram_tensor(f"in_{name}_dram", a.shape, _mybir.dt.from_np(a.dtype), kind="ExternalInput").ap())
    out = nc.dram_tensor("out_dram", inputs["x"].shape, _mybir.dt.float32, kind="ExternalOutput").ap()
    cond_resid_kernel(nc, *args, out)
    r = _run(nc, [arrays], core_ids=[0])
    return r.results[0]["out_dram"]
```
